# Optimizing a Trainium2 kernel written in Bass

```python
import numpy as np
import jax
import jax.numpy as jnp

def _softmax(x, axis=-1):
    return jax.nn.softmax(x, axis=axis)

def _gelu(x):
    return jax.nn.gelu(x, approximate=True)

def _silu(x):
    return jax.nn.silu(x)

def _sigmoid(x):
    return jax.nn.sigmoid(x)

def _layernorm(x, axis=-1, eps=1e-05):
    m = jnp.mean(x, axis=axis, keepdims=True)
    v = jnp.var(x, axis=axis, keepdims=True)
    return (x - m) / jnp.sqrt(v + eps)

def _scatter_add(tgt, idx, src, axis=0):
    return tgt.at[idx].add(src)

def _segment_sum(src, seg, n):
    return jax.ops.segment_sum(src, seg, n)
kernel_name = 'mk_adj_resnorm_d1_adj_r2_c579a3'

def setup_inputs(seed: int=0):
    np.random.seed(seed)
    _w = jnp.asarray

    def _rec_inputs():
        import jax
        import jax.numpy as jnp
        _gk = jax.random.key(seed)
        x = -0.0002928 + 1 * jax.random.normal(jax.random.fold_in(_gk, 1), (4096, 256), jnp.float32)
        _a = jax.random.bernoulli(jax.random.fold_in(_gk, 2), 0.00195312, (4096, 4096))
        _a = jnp.logical_or(_a, jnp.swapaxes(_a, -1, -2))
        _a = jnp.logical_or(_a, jnp.eye(4096, dtype=bool))
        _af = _a.astype(jnp.float32)
        _af = _af * jax.random.uniform(jax.random.fold_in(_gk, 3), (4096, 4096), jnp.float32, 0.05, 5.41998)
        adj = _af
        return (x, adj)
    x, adj = _rec_inputs()

    def _L0_gnn_setup():
        import jax, jax.numpy as jnp
        import numpy as np
        N = 4096
        D = 256
        EPS = 1e-12
        key = jax.random.key(seed)
        k1, k2 = jax.random.split(key)
        cur = jax.random.normal(k1, (N, D), dtype=jnp.float32)
        incidence_m = jax.random.normal(k2, (N, N), dtype=jnp.float32)
        return {'cur': cur, 'incidence_m': incidence_m}
    _L0_gnn_all = _L0_gnn_setup()
    _L0_gnn_in = {k: v for k, v in _L0_gnn_all.items() if k in ()}
    del _L0_gnn_all
    return {'x': x, 'adj': adj}

def reference(x, adj):
    import jax
    import jax.numpy as jnp

    def _L0_gnn_ref(cur, incidence_m):
        import jax, jax.numpy as jnp
        import numpy as np
        N = 4096
        D = 256
        EPS = 1e-12
        mask = incidence_m > 0
        head = jax.lax.stop_gradient(mask.astype(incidence_m.dtype))
        head = head / jnp.maximum(jnp.sqrt(jnp.sum(head * head, axis=-1, keepdims=True)), EPS)
        inc = incidence_m + head
        edge_fea = inc @ cur
        edge_degree = jnp.sum(inc, axis=-1, keepdims=True)
        return edge_fea / edge_degree
    x = _layernorm(x + _L0_gnn_ref(x, adj), axis=-1)
    return x

_drawn_inputs = setup_inputs


def setup_inputs(seed=0):
    import zlib

    import numpy as np

    out = dict(_drawn_inputs(seed))
    spreads = {}
    factors = {}
    for name, (base, spread) in spreads.items():
        noise = np.random.default_rng([zlib.crc32(name.encode()), seed]).standard_normal(out[name].shape)
        drawn = base * np.exp(spread * noise) if base else spread * noise
        out[name] = jnp.asarray(drawn.astype(out[name].dtype))
    for name, factor in factors.items():
        out[name] = (out[name] * factor).astype(out[name].dtype)
    return out
```

```python
import concourse.bass as bass
from concourse import mybir
from contextlib import ExitStack


def gnn_resnorm_kernel(nc: bass.Bass, x: bass.AP, adj: bass.AP, out: bass.AP):
    fp32 = mybir.dt.float32
    bf16 = mybir.dt.bfloat16
    ALU = mybir.AluOpType
    ACT = mybir.ActivationFunctionType

    P = 128
    N, D = x.shape
    TILES = N // P
    SQ = 32
    G = P // SQ
    COLS = N // G
    B = COLS // SQ
    EPS = 1e-5
    SIGN_SCALE = 2.0 ** 60
    SIGN_BIAS = -2.0 ** -90
    SLOT = 16 * G

    adj_v = adj.rearrange("(t q r) (g c) -> t g r q c", q=G, r=SQ, g=G)
    x_v = x.rearrange("(g b j) d -> g j b d", g=G, j=SQ)
    x_rows = x.rearrange("(t p) d -> t p d", p=P)
    out_rows = out.rearrange("(t p) d -> t p d", p=P)

    ctx = ExitStack()
    with ctx:
        def sb(name, shape, dt):
            return ctx.enter_context(nc.sbuf_tensor(name, shape, dt))

        def pb(name, shape, dt):
            return ctx.enter_context(nc.psum_tensor(name, shape, dt))

        def sem(name):
            return ctx.enter_context(nc.semaphore(name))

        raw = sb("raw", [P, 2, G, COLS], fp32)
        inc = sb("inc", [P, G, COLS], fp32)
        incT = sb("incT", [P, 2, B, G, SQ], fp32)
        xk = sb("xk", [P, B, D], fp32)
        xres = sb("xres", [P, 2, D], fp32)
        sign_out = sb("sign_out", [P, 2, COLS], bf16)
        sign_sum = sb("sign_sum", [P, 2, G], fp32)
        count = sb("count", [P, 2, G], fp32)
        norm = sb("norm", [P, 2, G], fp32)
        deg_part = sb("deg_part", [P, 2, G], fp32)
        half = sb("half", [P, G], fp32)
        minus_half = sb("minus_half", [P, 1], fp32)
        sign_bias = sb("sign_bias", [P, 1], fp32)
        quad_sum = sb("quad_sum", [P, P], fp32)
        own_quarter = sb("own_quarter", [P, G], fp32)
        deg_pick = sb("deg_pick", [P, G], fp32)
        deg = sb("deg", [P, 1], fp32)
        rdeg = sb("rdeg", [P, 1], fp32)
        y = sb("y", [P, 2, D], fp32)
        stats = sb("stats", [P, 6], fp32)
        stats_seen = sb("stats_seen", [P, 1], fp32)
        mean_var = sb("mean_var", [P, 2, 2], fp32)
        var_eps = sb("var_eps", [P, 2], fp32)
        rstd = sb("rstd", [P, 2], fp32)
        result = sb("result", [P, 2, D], fp32)

        scaled = [pb(f"scaled{i}", [P, COLS], fp32) for i in range(2)]
        edge = [pb(f"edge{i}", [P, 512], fp32) for i in range(2)]
        count_ps = pb("count_ps", [P, 512], fp32)
        deg_ps = pb("deg_ps", [P, 512], fp32)

        raw_in = [[sem(f"raw_in{s}{q}") for q in range(G)] for s in range(2)]
        xk_in = sem("xk_in")
        xres_in = [sem(f"xres_in{s}") for s in range(2)]
        consts_ready = sem("consts_ready")
        const_step = sem("const_step")
        signs_ready = sem("signs_ready")
        count_summed = sem("count_summed")
        count_ready = sem("count_ready")
        norm_ready = sem("norm_ready")
        scaled_ready = sem("scaled_ready")
        inc_ready = sem("inc_ready")
        incT_ready = sem("incT_ready")
        edge_ready = sem("edge_ready")
        deg_summed = sem("deg_summed")
        dve_step = sem("dve_step")
        y_ready = sem("y_ready")
        var_ready = sem("var_ready")
        rstd_ready = sem("rstd_ready")
        result_ready = sem("result_ready")
        stored = [sem(f"stored{s}") for s in range(2)]

        block = ctx.enter_context(nc.Block())

        PAIRS = TILES // 2

        @block.sync
        def _(sp):
            def load_quarter(t, s, u, q, reuse):
                if reuse:
                    sp.wait_ge(inc_ready, G * t - 2 * G + q + 1)
                for g in range(G):
                    sp.dma_start(raw[SQ * g:SQ * (g + 1), s, q, :], adj_v[t, g, :, q, :]).then_inc(raw_in[s][q], 16)

            def load_residual(t, s, reuse):
                if reuse:
                    sp.wait_ge(y_ready, t - 1)
                sp.dma_start(xres[:, s, :], x_rows[t]).then_inc(xres_in[s], 16)

            def store(t, s):
                sp.wait_ge(result_ready, t + 1)
                sp.dma_start(out_rows[t], result[:, s, :]).then_inc(stored[s], 16)

            for s in range(2):
                for q in range(G):
                    load_quarter(s, s, 0, q, False)
                load_residual(s, s, False)
            with sp.Fori(1, PAIRS) as u:
                for s in range(2):
                    t = 2 * u + s
                    for q in range(G):
                        load_quarter(t, s, u, q, True)
                    store(t - 2, s)
                    load_residual(t, s, True)
            for s in range(2):
                store(TILES - 2 + s, s)
            for s in range(2):
                sp.wait_ge(stored[s], 16 * PAIRS)

        @block.scalar
        def _(act):
            act.wait_ge(consts_ready, 1)

            def sign_quarter(t, s, u, q, reuse):
                act.wait_ge(raw_in[s][q], (u + 1) * SLOT)
                if reuse or q >= 2:
                    act.wait_ge(signs_ready, G * t + q - 1)
                nc.scalar.activation(sign_out[:, q % 2, :], raw[:, s, q, :], ACT.Sign, scale=SIGN_SCALE,
                                     bias=sign_bias[:, 0:1], accum_out=sign_sum[:, s, q:q + 1]).then_inc(signs_ready, 1)

            def scale_quarter(t, s, q, reuse):
                if q == 0:
                    act.wait_ge(norm_ready, t + 1)
                if reuse or q >= 2:
                    act.wait_ge(inc_ready, G * t + q - 1)
                nc.scalar.mul(scaled[q % 2][:, :], raw[:, s, q, :], norm[:, s, q:q + 1]).then_inc(scaled_ready, 1)

            for g in range(G):
                act.dma_start(xk[SQ * g:SQ * (g + 1), :, :], x_v[g]).then_inc(xk_in, 16)
            for q in range(G):
                sign_quarter(0, 0, 0, q, False)

            def tile(t, s, u, u_next, reuse, more=True):
                for q in range(G):
                    scale_quarter(t, s, q, reuse)
                    if more:
                        sign_quarter(t + 1, 1 - s, u_next, q, True)

            tile(0, 0, 0, 0, False)
            tile(1, 1, 0, 1, True)
            with act.Fori(1, PAIRS - 1) as u:
                tile(2 * u, 0, u, u, True)
                tile(2 * u + 1, 1, u, u + 1, True)
            tile(TILES - 2, 0, PAIRS - 1, PAIRS - 1, True)
            tile(TILES - 1, 1, PAIRS - 1, PAIRS, True, more=False)

        @block.gpsimd
        def _(pool):
            nc.gpsimd.memset(quad_sum[:, :], 0.0).then_inc(const_step, 1)
            nc.gpsimd.memset(half[:, :], 0.5)
            nc.gpsimd.memset(minus_half[:, :], -0.5)
            nc.gpsimd.memset(sign_bias[:, :], SIGN_BIAS)
            nc.gpsimd.memset(own_quarter[:, :], 0.0).then_inc(const_step, 1)
            pool.wait_ge(const_step, 2)
            for g in range(G):
                v = quad_sum[:, :].rearrange("p (g j) -> p g j", g=G)
                nc.gpsimd.affine_select(out=v, in_=v, compare_op=ALU.not_equal, fill=0.5, base=-SQ * g,
                                        pattern=[[0, G], [-1, SQ]], channel_multiplier=1).then_inc(const_step, 1)
                pool.wait_ge(const_step, 3 + g)
            for g in range(G):
                last = nc.gpsimd.memset(own_quarter[SQ * g:SQ * (g + 1), g:g + 1], 2.0)
            last.then_inc(consts_ready, 1)

            def norm_of(t, s):
                pool.wait_ge(count_ready, t + 1)
                nc.gpsimd.tensor_tensor(norm[:, s, :], count[:, s, :], half[:, :], ALU.pow).then_inc(norm_ready, 1)

            def rstd_of(t, s):
                pool.wait_ge(var_ready, t + 1)
                nc.gpsimd.tensor_tensor(rstd[:, s:s + 1], var_eps[:, s:s + 1], minus_half[:, :],
                                        ALU.pow).then_inc(rstd_ready, 1)

            norm_of(0, 0)
            norm_of(1, 1)
            with pool.Fori(1, PAIRS) as u:
                for s in range(2):
                    t = 2 * u + s
                    rstd_of(t - 2, s)
                    norm_of(t, s)
            for s in range(2):
                rstd_of(TILES - 2 + s, s)

        @block.vector
        def _(dve):
            def count_of(t, s):
                dve.wait_ge(count_summed, t + 1)
                nc.vector.tensor_scalar(count[:, s, :], count_ps[:, 0:G], float(N // 2), 1.0,
                                        ALU.add, ALU.max).then_inc(count_ready, 1)

            def inc_quarter(t, s, q, reuse):
                if reuse:
                    dve.wait_ge(incT_ready, G * t - G + q + 1)
                dve.wait_ge(scaled_ready, G * t + q + 1)
                nc.vector.scalar_tensor_tensor(inc[:, q, :], raw[:, s, q, :], 0.0, scaled[q % 2][:, :],
                                               ALU.is_gt, ALU.add,
                                               accum_out=deg_part[:, s, q:q + 1]).then_inc(inc_ready, 1)

            def transpose_quarter(t, s, q, reuse):
                if reuse and q == 0:
                    dve.wait_ge(edge_ready, t - 1)
                dve.wait_ge(inc_ready, G * t + q + 1)
                nc.vector.transpose(incT[:, s, :, q, :],
                                    inc[:, q, :].rearrange("p (b j) -> p b j", j=SQ)).then_inc(incT_ready, 1)



            def residual(t, s, u):
                def step(ins, k):
                    ins.then_inc(dve_step, 1)
                    dve.wait_ge(dve_step, STEPS * t + k)
                dve.wait_ge(deg_summed, t + 1)
                step(nc.vector.scalar_tensor_tensor(deg_pick[:, :], deg_ps[:, 0:G], 1.0, own_quarter[:, :],
                                                    ALU.mult, ALU.mult, accum_out=deg[:, :]), 1)
                step(nc.vector.reciprocal(rdeg[:, :], deg[:, :]), 2)
                dve.wait_ge(xres_in[s], 16 * (u + 1))
                nc.vector.scalar_tensor_tensor(y[:, s, :], edge[s][:, 0:D], rdeg[:, :], xres[:, s, :],
                                               ALU.mult, ALU.add).then_inc(y_ready, 1)
                dve.wait_ge(y_ready, t + 1)
                step(nc.vector.bn_stats(stats[:, :], y[:, s, :]), 3)
                nc.vector.tensor_copy(stats_seen[:, :], stats[:, 0:1])
                step(nc.vector.bn_aggr(mean_var[:, s, :], stats[:, :]), 4)
                nc.vector.tensor_scalar(var_eps[:, s:s + 1], mean_var[:, s, 1:2], EPS, None,
                                        ALU.add).then_inc(var_ready, 1)

            def normalise(t, s, u, reuse):
                dve.wait_ge(rstd_ready, t + 1)
                if reuse:
                    dve.wait_ge(stored[s], 16 * u)
                nc.vector.tensor_scalar(result[:, s, :], y[:, s, :], mean_var[:, s, 0:1], rstd[:, s:s + 1],
                                        ALU.subtract, ALU.mult).then_inc(result_ready, 1)

            STEPS = 4
            count_of(0, 0)

            def tile(t, s, u, u_before, reuse, before=True, count_next=True, reuse_before=True, reuse_inc=True):
                inc_quarter(t, s, 0, reuse_inc)
                inc_quarter(t, s, 1, reuse_inc)
                transpose_quarter(t, s, 0, reuse)
                inc_quarter(t, s, 2, reuse_inc)
                transpose_quarter(t, s, 1, reuse)
                inc_quarter(t, s, 3, reuse_inc)
                if count_next:
                    count_of(t + 1, 1 - s)
                transpose_quarter(t, s, 2, reuse)
                transpose_quarter(t, s, 3, reuse)
                if before:
                    residual(t - 1, 1 - s, u_before)
                    normalise(t - 1, 1 - s, u_before, reuse_before)

            tile(0, 0, 0, 0, False, before=False, reuse_inc=False)
            tile(1, 1, 0, 0, False, reuse_before=False)
            tile(2, 0, 1, 0, True, reuse_before=False)
            tile(3, 1, 1, 1, True)
            with dve.Fori(2, PAIRS - 1) as u:
                tile(2 * u, 0, u, u - 1, True)
                tile(2 * u + 1, 1, u, u, True)
            tile(TILES - 2, 0, PAIRS - 1, PAIRS - 2, True)
            tile(TILES - 1, 1, PAIRS - 1, PAIRS - 1, True, count_next=False)
            residual(TILES - 1, 1, PAIRS - 1)
            normalise(TILES - 1, 1, PAIRS - 1, True)

        @block.tensor
        def _(pe):
            def sum_counts(t, s, reuse):
                pe.wait_ge(signs_ready, G * t + G)
                if reuse:
                    pe.wait_ge(count_ready, t)
                nc.tensor.matmul(count_ps[:, 0:G], quad_sum[:, :], sign_sum[:, s, :],
                                 start=True, stop=True).then_inc(count_summed, 1)

            def products(t, s, b0, b1, reuse=False):
                if b0 == 0:
                    pe.wait_ge(incT_ready, G * t + G)
                    if reuse:
                        pe.wait_ge(y_ready, t - 1)
                for b in range(b0, b1):
                    last = nc.tensor.matmul(edge[s][:, 0:D], incT[:, s, b, :, :].rearrange("p q j -> p (q j)"),
                                            xk[:, b, :], start=(b == 0), stop=(b == B - 1))
                if b1 == B:
                    last.then_inc(edge_ready, 1)

            def sum_degrees(t, s, reuse):
                if reuse:
                    pe.wait_ge(dve_step, 4 * t - 3)
                nc.tensor.matmul(deg_ps[:, 0:G], quad_sum[:, :], deg_part[:, s, :],
                                 start=True, stop=True).then_inc(deg_summed, 1)

            pe.wait_ge(consts_ready, 1)
            sum_counts(0, 0, False)
            sum_counts(1, 1, True)
            pe.wait_ge(xk_in, 16 * G)

            def tile(t, s, reuse, counts=True, first=False):
                products(t, s, 0, B // 2, reuse)
                if counts:
                    sum_counts(t + 2, s, True)
                products(t, s, B // 2, B)
                sum_degrees(t, s, not first)

            tile(0, 0, False, first=True)
            tile(1, 1, False)
            with pe.Fori(1, PAIRS - 1) as u:
                for s in range(2):
                    tile(2 * u + s, s, True)
            tile(TILES - 2, 0, True, counts=False)
            tile(TILES - 1, 1, True, counts=False)


_INS = ["x", "adj"]


def kernel(**inputs):
    import numpy as _np
    import concourse.bacc as _bacc
    from concourse import mybir as _mybir
    from concourse.bass_utils import run_bass_kernel_spmd as _run

    nc = _bacc.Bacc("TRN2", target_bir_lowering=False, num_devices=1)
    arrays, args = {}, []
    for name in _INS:
        a = _np.ascontiguousarray(inputs[name])
        arrays[f"in_{name}_dram"] = a
        args.append(nc.dram_tensor(f"in_{name}_dram", a.shape, _mybir.dt.from_np(a.dtype), kind="ExternalInput").ap())
    shape = inputs["x"].shape
    args.append(nc.dram_tensor("out_0_dram", shape, _mybir.dt.float32, kind="ExternalOutput").ap())
    gnn_resnorm_kernel(nc, *args)
    r = _run(nc, [arrays], core_ids=[0])
    return r.results[0]["out_0_dram"]
```

```python
import concourse.bass as bass
from concourse import mybir
from contextlib import ExitStack


def gnn_resnorm_kernel(nc: bass.Bass, x: bass.AP, adj: bass.AP, out: bass.AP):
    fp32 = mybir.dt.float32
    fp32r = mybir.dt.float32r
    bf16 = mybir.dt.bfloat16
    ALU = mybir.AluOpType
    ACT = mybir.ActivationFunctionType

    P = 128
    N, D = x.shape
    TILES = N // P
    SQ = 32
    G = P // SQ
    COLS = N // G
    B = COLS // SQ
    EPS = 1e-5
    SIGN_SCALE = 2.0 ** 60
    SIGN_BIAS = -2.0 ** -90
    SLOT = 16 * G

    adj_v = adj.rearrange("(t q r) (g c) -> t g r q c", q=G, r=SQ, g=G)
    x_v = x.rearrange("(g b j) d -> g j b d", g=G, j=SQ)
    x_rows = x.rearrange("(t p) d -> t p d", p=P)
    out_rows = out.rearrange("(t p) d -> t p d", p=P)

    ctx = ExitStack()
    with ctx:
        def sb(name, shape, dt):
            return ctx.enter_context(nc.sbuf_tensor(name, shape, dt))

        def pb(name, shape, dt):
            return ctx.enter_context(nc.psum_tensor(name, shape, dt))

        def sem(name):
            return ctx.enter_context(nc.semaphore(name))

        raw = sb("raw", [P, 2, G, COLS], fp32)
        inc = sb("inc", [P, G, COLS], fp32)
        incT = sb("incT", [P, G, B, SQ], fp32)
        inc_hi = sb("inc_hi", [P, 2, B, G, SQ], fp32r)
        inc_lo = sb("inc_lo", [P, 2, B, G, SQ], fp32r)
        x_split = sb("x_split", [P, B, 2, D], fp32r)
        xres = sb("xres", [P, 2, D], fp32)
        sign_out = sb("sign_out", [P, COLS], bf16)
        sign_sum = sb("sign_sum", [P, 2, G], fp32)
        count = sb("count", [P, 2, G], fp32)
        norm = sb("norm", [P, 2, G], fp32)
        deg_part = sb("deg_part", [P, 2, G], fp32)
        half = sb("half", [P, G], fp32)
        quarter = sb("quarter", [P, 1], fp32)
        minus_half = sb("minus_half", [P, 1], fp32)
        sign_bias = sb("sign_bias", [P, 1], fp32)
        quad_sum = sb("quad_sum", [P, P], fp32)
        own_quarter = sb("own_quarter", [P, G], fp32)
        deg_pick = sb("deg_pick", [P, G], fp32)
        deg = sb("deg", [P, 1], fp32)
        rdeg = sb("rdeg", [P, 1], fp32)
        y_main = sb("y_main", [P, D], fp32)
        y = sb("y", [P, 2, D], fp32)
        stats = sb("stats", [P, 6], fp32)
        stats_seen = sb("stats_seen", [P, 1], fp32)
        mean_var = sb("mean_var", [P, 2, 2], fp32)
        var_eps = sb("var_eps", [P, 2], fp32)
        rstd = sb("rstd", [P, 2], fp32)
        result = sb("result", [P, 2, D], fp32)

        scaled = [pb(f"scaled{i}", [P, COLS], fp32) for i in range(2)]
        edge = [pb(f"edge{i}", [P, 512], fp32) for i in range(2)]
        count_ps = pb("count_ps", [P, 512], fp32)
        deg_ps = pb("deg_ps", [P, 512], fp32)

        raw_in = [[sem(f"raw_in{s}{q}") for q in range(G)] for s in range(2)]
        x_in = [sem(f"x_in{i}") for i in range(2)]
        x_hi_ready = sem("x_hi_ready")
        x_lo_ready = sem("x_lo_ready")
        xres_in = [sem(f"xres_in{s}") for s in range(2)]
        consts_ready = sem("consts_ready")
        const_step = sem("const_step")
        signs_ready = sem("signs_ready")
        count_summed = sem("count_summed")
        count_ready = sem("count_ready")
        norm_ready = sem("norm_ready")
        scaled_ready = sem("scaled_ready")
        inc_ready = sem("inc_ready")
        incT_ready = sem("incT_ready")
        hi_ready = sem("hi_ready")
        hi_pool_ready = sem("hi_pool_ready")
        lo_ready = sem("lo_ready")
        edge_ready = sem("edge_ready")
        deg_summed = sem("deg_summed")
        dve_step = sem("dve_step")
        y_ready = sem("y_ready")
        var_ready = sem("var_ready")
        rstd_ready = sem("rstd_ready")
        result_ready = sem("result_ready")
        stored = [sem(f"stored{s}") for s in range(2)]

        block = ctx.enter_context(nc.Block())

        PAIRS = TILES // 2
        XB = B // 8
        X_CHUNKS = B // XB
        ACT_HI = 2
        STEPS = 5

        def x_stage(c):
            return incT[:, 2 + c % 2, :, :].rearrange("p b j -> p (b j)").rearrange("p (b d) -> p b d", d=D)

        def hi_of(s, q):
            return inc_hi[:, s, :, q, :]

        @block.sync
        def _(sp):
            def load_quarter(t, s, q, reuse):
                if reuse:
                    sp.wait_ge(inc_ready, G * t - 2 * G + q + 1)
                for g in range(G):
                    sp.dma_start(raw[SQ * g:SQ * (g + 1), s, q, :], adj_v[t, g, :, q, :]).then_inc(raw_in[s][q], 16)

            def load_residual(t, s, reuse):
                if reuse:
                    sp.wait_ge(y_ready, t - 1)
                sp.dma_start(xres[:, s, :], x_rows[t]).then_inc(xres_in[s], 16)

            def store(t, s):
                sp.wait_ge(result_ready, t + 1)
                sp.dma_start(out_rows[t], result[:, s, :]).then_inc(stored[s], 16)

            for s in range(2):
                for q in range(G):
                    load_quarter(s, s, q, False)
            for s in range(2):
                for q in range(G):
                    load_quarter(2 + s, s, q, True)
                load_residual(s, s, False)
            with sp.Fori(2, PAIRS) as u:
                for s in range(2):
                    t = 2 * u + s
                    for q in range(G):
                        load_quarter(t, s, q, True)
                    store(t - 4, s)
                    load_residual(t - 2, s, True)
            for s in range(2):
                store(TILES - 4 + s, s)
                load_residual(TILES - 2 + s, s, True)
            for s in range(2):
                store(TILES - 2 + s, s)
            for s in range(2):
                sp.wait_ge(stored[s], 16 * PAIRS)

        @block.scalar
        def _(act):
            for c in range(X_CHUNKS):
                if c >= 2:
                    act.wait_ge(x_lo_ready, c - 1)
                for g in range(G):
                    act.dma_start(x_stage(c)[SQ * g:SQ * (g + 1)],
                                  x_v[g, :, XB * c:XB * (c + 1), :]).then_inc(x_in[c % 2], 16)

            def sign_quarter(t, s, u, q, first=False):
                act.wait_ge(raw_in[s][q], (u + 1) * SLOT)
                if not first:
                    act.wait_ge(signs_ready, G * t + q)
                nc.scalar.activation(sign_out[:, :], raw[:, s, q, :], ACT.Sign, scale=SIGN_SCALE,
                                     bias=sign_bias[:, 0:1], accum_out=sign_sum[:, s, q:q + 1]).then_inc(signs_ready, 1)

            def scale_quarter(t, s, q, reuse):
                if q == 0:
                    act.wait_ge(norm_ready, t + 1)
                if reuse or q >= 2:
                    act.wait_ge(inc_ready, G * t + q - 1)
                nc.scalar.mul(scaled[q % 2][:, :], raw[:, s, q, :], norm[:, s, q:q + 1]).then_inc(scaled_ready, 1)

            def round_quarter(t, s, q, reuse):
                if reuse:
                    act.wait_ge(edge_ready, t - 1)
                act.wait_ge(incT_ready, G * t + q + 1)
                nc.scalar.copy(hi_of(s, q), incT[:, q, :, :]).then_inc(hi_ready, 1)

            act.wait_ge(consts_ready, 1)
            for q in range(G):
                sign_quarter(0, 0, 0, q, first=(q == 0))

            def tile(t, s, u_next, reuse_scaled=True, reuse_hi=True, more=True):
                order = ["t0", "s0", "t1", "s1", "s2", "t2", "s3", "h0", "t3", "h1"]
                for step in order:
                    q = int(step[1])
                    if step[0] == "t":
                        scale_quarter(t, s, q, reuse_scaled)
                    elif step[0] == "h":
                        round_quarter(t, s, q, reuse_hi)
                    elif more:
                        sign_quarter(t + 1, 1 - s, u_next, q)

            tile(0, 0, 0, reuse_scaled=False, reuse_hi=False)
            tile(1, 1, 1, reuse_hi=False)
            with act.Fori(1, PAIRS - 1) as u:
                tile(2 * u, 0, u)
                tile(2 * u + 1, 1, u + 1)
            tile(TILES - 2, 0, PAIRS - 1)
            tile(TILES - 1, 1, PAIRS, more=False)

        @block.gpsimd
        def _(pool):
            nc.gpsimd.memset(quad_sum[:, :], 0.0).then_inc(const_step, 1)
            nc.gpsimd.memset(half[:, :], 0.5)
            nc.gpsimd.memset(minus_half[:, :], -0.5)
            nc.gpsimd.memset(sign_bias[:, :], SIGN_BIAS)
            nc.gpsimd.memset(own_quarter[:, :], 0.0).then_inc(const_step, 1)
            pool.wait_ge(const_step, 2)
            for g in range(G):
                v = quad_sum[:, :].rearrange("p (g j) -> p g j", g=G)
                nc.gpsimd.affine_select(out=v, in_=v, compare_op=ALU.not_equal, fill=0.5, base=-SQ * g,
                                        pattern=[[0, G], [-1, SQ]], channel_multiplier=1).then_inc(const_step, 1)
                pool.wait_ge(const_step, 3 + g)
            for g in range(G):
                last = nc.gpsimd.memset(own_quarter[SQ * g:SQ * (g + 1), g:g + 1], 2.0)
            last.then_inc(consts_ready, 1)

            def norm_of(t, s):
                pool.wait_ge(count_ready, t + 1)
                nc.gpsimd.tensor_tensor(norm[:, s, :], count[:, s, :], half[:, :], ALU.pow).then_inc(norm_ready, 1)

            def rstd_of(t, s):
                pool.wait_ge(var_ready, t + 1)
                nc.gpsimd.tensor_tensor(rstd[:, s:s + 1], var_eps[:, s:s + 1], minus_half[:, :],
                                        ALU.pow).then_inc(rstd_ready, 1)

            def round_quarter(t, s, q, reuse):
                if reuse:
                    pool.wait_ge(edge_ready, t - 1)
                pool.wait_ge(incT_ready, G * t + q + 1)
                nc.gpsimd.tensor_tensor(quarter[:, :], half[:, 0:1], half[:, 0:1], ALU.mult)
                nc.gpsimd.tensor_scalar(hi_of(s, q), incT[:, q, :, :], 1.0, 1.0, ALU.mult, ALU.mult).then_inc(hi_pool_ready, 1)

            def low_quarter(t, s, q):
                if q < ACT_HI:
                    pool.wait_ge(hi_ready, ACT_HI * t + q + 1)
                else:
                    pool.wait_ge(hi_pool_ready, (G - ACT_HI) * t + q - ACT_HI + 1)
                nc.gpsimd.tensor_tensor(inc_lo[:, s, :, q, :], incT[:, q, :, :], hi_of(s, q).bitcast(fp32),
                                        ALU.subtract).then_inc(lo_ready, 1)

            norm_of(0, 0)

            def tile(t, s, reuse=True, more=True):
                low_quarter(t, s, 0)
                if reuse:
                    rstd_of(t - 2, s)
                low_quarter(t, s, 1)
                round_quarter(t, s, 2, reuse)
                if more:
                    norm_of(t + 1, 1 - s)
                low_quarter(t, s, 2)
                round_quarter(t, s, 3, reuse)
                low_quarter(t, s, 3)

            tile(0, 0, reuse=False)
            tile(1, 1, reuse=False)
            with pool.Fori(1, PAIRS - 1) as u:
                tile(2 * u, 0)
                tile(2 * u + 1, 1)
            tile(TILES - 2, 0)
            tile(TILES - 1, 1, more=False)
            for s in range(2):
                rstd_of(TILES - 2 + s, s)

        @block.vector
        def _(dve):
            for c in range(X_CHUNKS):
                dve.wait_ge(x_in[c % 2], SLOT * (c // 2 + 1))
                hi = x_split[:, XB * c:XB * (c + 1), 0, :]
                nc.vector.tensor_copy(hi, x_stage(c)).then_inc(x_hi_ready, 1)
                dve.wait_ge(x_hi_ready, c + 1)
                nc.vector.tensor_tensor(x_split[:, XB * c:XB * (c + 1), 1, :], x_stage(c), hi.bitcast(fp32),
                                        ALU.subtract).then_inc(x_lo_ready, 1)

            def count_of(t, s):
                dve.wait_ge(count_summed, t + 1)
                nc.vector.tensor_scalar(count[:, s, :], count_ps[:, 0:G], float(N // 2), 1.0,
                                        ALU.add, ALU.max).then_inc(count_ready, 1)

            def inc_quarter(t, s, q, reuse, reuse_deg):
                if reuse:
                    dve.wait_ge(incT_ready, G * t - G + q + 1)
                if reuse_deg and q == 0:
                    dve.wait_ge(deg_summed, t - 1)
                dve.wait_ge(scaled_ready, G * t + q + 1)
                nc.vector.scalar_tensor_tensor(inc[:, q, :], raw[:, s, q, :], 0.0, scaled[q % 2][:, :],
                                               ALU.is_gt, ALU.add,
                                               accum_out=deg_part[:, s, q:q + 1]).then_inc(inc_ready, 1)

            def transpose_quarter(t, s, q, reuse):
                if reuse:
                    dve.wait_ge(lo_ready, G * t - G + q + 1)
                elif q == 2:
                    dve.wait_ge(x_lo_ready, X_CHUNKS)
                dve.wait_ge(inc_ready, G * t + q + 1)
                nc.vector.transpose(incT[:, q, :, :].rearrange("p b j -> p (b j)"), inc[:, q, :]).then_inc(incT_ready, 1)

            def residual(t, s, u):
                def step(ins, k):
                    ins.then_inc(dve_step, 1)
                    dve.wait_ge(dve_step, STEPS * t + k)
                dve.wait_ge(deg_summed, t + 1)
                step(nc.vector.scalar_tensor_tensor(deg_pick[:, :], deg_ps[:, 0:G], 1.0, own_quarter[:, :],
                                                    ALU.mult, ALU.mult, accum_out=deg[:, :]), 1)
                step(nc.vector.reciprocal(rdeg[:, :], deg[:, :]), 2)
                dve.wait_ge(edge_ready, t + 1)
                dve.wait_ge(xres_in[s], 16 * (u + 1))
                step(nc.vector.scalar_tensor_tensor(y_main[:, :], edge[s][:, D:2 * D], rdeg[:, :], xres[:, s, :],
                                                    ALU.mult, ALU.add), 3)
                nc.vector.scalar_tensor_tensor(y[:, s, :], edge[s][:, 0:D], rdeg[:, :], y_main[:, :],
                                               ALU.mult, ALU.add).then_inc(y_ready, 1)
                dve.wait_ge(y_ready, t + 1)
                step(nc.vector.bn_stats(stats[:, :], y[:, s, :]), 4)
                nc.vector.tensor_copy(stats_seen[:, :], stats[:, 0:1])
                step(nc.vector.bn_aggr(mean_var[:, s, :], stats[:, :]), 5)
                nc.vector.tensor_scalar(var_eps[:, s:s + 1], mean_var[:, s, 1:2], EPS, None,
                                        ALU.add).then_inc(var_ready, 1)

            def normalise(t, s, u, reuse):
                dve.wait_ge(rstd_ready, t + 1)
                if reuse:
                    dve.wait_ge(stored[s], 16 * u)
                nc.vector.tensor_scalar(result[:, s, :], y[:, s, :], mean_var[:, s, 0:1], rstd[:, s:s + 1],
                                        ALU.subtract, ALU.mult).then_inc(result_ready, 1)

            count_of(0, 0)

            def tile(t, s, u_before, reuse=True, before=True, reuse_before=True, more=True):
                inc_quarter(t, s, 0, reuse, before)
                inc_quarter(t, s, 1, reuse, before)
                transpose_quarter(t, s, 0, reuse)
                inc_quarter(t, s, 2, reuse, before)
                transpose_quarter(t, s, 1, reuse)
                if before:
                    residual(t - 2, s, u_before)
                inc_quarter(t, s, 3, reuse, before)
                transpose_quarter(t, s, 2, reuse)
                if more:
                    count_of(t + 1, 1 - s)
                transpose_quarter(t, s, 3, reuse)
                if before:
                    normalise(t - 2, s, u_before, reuse_before)

            tile(0, 0, 0, reuse=False, before=False)
            tile(1, 1, 0, before=False)
            tile(2, 0, 0, reuse_before=False)
            tile(3, 1, 0, reuse_before=False)
            with dve.Fori(2, PAIRS - 1) as u:
                tile(2 * u, 0, u - 1)
                tile(2 * u + 1, 1, u - 1)
            tile(TILES - 2, 0, PAIRS - 2)
            tile(TILES - 1, 1, PAIRS - 2, more=False)
            for s in range(2):
                residual(TILES - 2 + s, s, PAIRS - 1)
                normalise(TILES - 2 + s, s, PAIRS - 1, True)

        @block.tensor
        def _(pe):
            def sum_counts(t, s, reuse):
                pe.wait_ge(signs_ready, G * t + G)
                if reuse:
                    pe.wait_ge(count_ready, t)
                nc.tensor.matmul(count_ps[:, 0:G], quad_sum[:, :], sign_sum[:, s, :],
                                 start=True, stop=True).then_inc(count_summed, 1)

            def products(t, s, b0, b1, reuse=False):
                if b0 == 0:
                    pe.wait_ge(lo_ready, G * t + G)
                    if reuse:
                        pe.wait_ge(y_ready, t - 1)
                for b in range(b0, b1):
                    nc.tensor.matmul(edge[s][:, :], inc_hi[:, s, b, :, :].rearrange("p q j -> p (q j)"),
                                     x_split[:, b, :, :].rearrange("p h d -> p (h d)"), start=(b == 0), stop=False)
                    last = nc.tensor.matmul(edge[s][:, D:2 * D], inc_lo[:, s, b, :, :].rearrange("p q j -> p (q j)"),
                                            x_split[:, b, 0, :], start=False, stop=(b == B - 1))
                if b1 == B:
                    last.then_inc(edge_ready, 1)

            def sum_degrees(t, s, reuse):
                if reuse:
                    pe.wait_ge(dve_step, STEPS * t - STEPS + 1)
                nc.tensor.matmul(deg_ps[:, 0:G], quad_sum[:, :], deg_part[:, s, :],
                                 start=True, stop=True).then_inc(deg_summed, 1)

            pe.wait_ge(consts_ready, 1)
            sum_counts(0, 0, False)
            sum_counts(1, 1, True)
            pe.wait_ge(x_lo_ready, X_CHUNKS)

            COUNTS_AT = B // 2
            DEGREES_AT = COUNTS_AT + 4

            def tile(t, s, reuse=True, counts=True, first=False):
                products(t, s, 0, COUNTS_AT, reuse)
                if counts:
                    sum_counts(t + 2, s, True)
                products(t, s, COUNTS_AT, DEGREES_AT)
                sum_degrees(t, s, not first)
                products(t, s, DEGREES_AT, B)

            tile(0, 0, reuse=False, first=True)
            tile(1, 1, reuse=False)
            with pe.Fori(1, PAIRS - 1) as u:
                for s in range(2):
                    tile(2 * u + s, s)
            tile(TILES - 2, 0, counts=False)
            tile(TILES - 1, 1, counts=False)


_INS = ["x", "adj"]


def kernel(**inputs):
    import numpy as _np
    import concourse.bacc as _bacc
    from concourse import mybir as _mybir
    from concourse.bass_utils import run_bass_kernel_spmd as _run

    nc = _bacc.Bacc("TRN2", target_bir_lowering=False, num_devices=1)
    arrays, args = {}, []
    for name in _INS:
        a = _np.ascontiguousarray(inputs[name])
        arrays[f"in_{name}_dram"] = a
        args.append(nc.dram_tensor(f"in_{name}_dram", a.shape, _mybir.dt.from_np(a.dtype), kind="ExternalInput").ap())
    shape = inputs["x"].shape
    args.append(nc.dram_tensor("out_0_dram", shape, _mybir.dt.float32, kind="ExternalOutput").ap())
    gnn_resnorm_kernel(nc, *args)
    r = _run(nc, [arrays], core_ids=[0])
    return r.results[0]["out_0_dram"]
```

```python
import concourse.bass as bass
from concourse import mybir
from contextlib import ExitStack


def gnn_resnorm_kernel(nc: bass.Bass, x: bass.AP, adj: bass.AP, out: bass.AP):
    fp32 = mybir.dt.float32
    fp32r = mybir.dt.float32r
    bf16 = mybir.dt.bfloat16
    ALU = mybir.AluOpType
    ACT = mybir.ActivationFunctionType

    P = 128
    N, D = x.shape
    TILES = N // P
    SQ = 32
    G = P // SQ
    COLS = N // G
    B = COLS // SQ
    NATIVE = 6
    SPLIT = B - NATIVE
    EPS = 1e-5
    SIGN_SCALE = 2.0 ** 60
    SIGN_BIAS = -2.0 ** -90
    X_CHUNK = 16 * G

    adj_v = adj.rearrange("(t q r) (g c) -> t g r q c", q=G, r=SQ, g=G)
    x_v = x.rearrange("(g b j) d -> g j b d", g=G, j=SQ)
    x_rows = x.rearrange("(t p) d -> t p d", p=P)
    out_rows = out.rearrange("(t p) d -> t p d", p=P)

    ctx = ExitStack()
    with ctx:
        def sb(name, shape, dt):
            return ctx.enter_context(nc.sbuf_tensor(name, shape, dt))

        def pb(name, shape, dt):
            return ctx.enter_context(nc.psum_tensor(name, shape, dt))

        def sem(name):
            return ctx.enter_context(nc.semaphore(name))

        raw = sb("raw", [P, 2, G, COLS], fp32)
        inc = sb("inc", [P, G, COLS], fp32)
        incT = sb("incT", [P, 2, B, G, SQ], fp32)
        inc_hi = sb("inc_hi", [P, 2, SPLIT, G, SQ], fp32r)
        inc_lo = sb("inc_lo", [P, 2, SPLIT, G, SQ], fp32r)
        x_split = sb("x_split", [P, SPLIT, 2, D], fp32r)
        x_native = sb("x_native", [P, NATIVE, D], fp32)
        rows = sb("rows", [P, max(7, SPLIT - B // 2), D], fp32)
        xres = rows[:, 0:2, :]
        sign_out = sb("sign_out", [P, COLS], bf16)
        part_sums = sb("part_sums", [P, 2, 2, G], fp32)
        count = sb("count", [P, 2, G], fp32)
        norm = sb("norm", [P, 2, G], fp32)
        half = sb("half", [P, G], fp32)
        minus_half = sb("minus_half", [P, 1], fp32)
        sign_bias = sb("sign_bias", [P, 1], fp32)
        table_load = sb("table_load", [P, 1], fp32)
        quad_sum = sb("quad_sum", [P, P], fp32)
        own_quarter = sb("own_quarter", [P, G], fp32)
        deg_pick = sb("deg_pick", [P, G], fp32)
        deg = sb("deg", [P, 1], fp32)
        rdeg = sb("rdeg", [P, 1], fp32)
        y_main = rows[:, 2, :]
        y = rows[:, 3:5, :]
        stats = sb("stats", [P, 6], fp32)
        stats_seen = sb("stats_seen", [P, 1], fp32)
        mean_var = sb("mean_var", [P, 2, 2], fp32)
        var_eps = sb("var_eps", [P, 2], fp32)
        rstd = sb("rstd", [P, 2], fp32)
        result = rows[:, 5:7, :]

        scaled = [pb(f"scaled{i}", [P, COLS], fp32) for i in range(2)]
        edge = [pb(f"edge{i}", [P, 512], fp32) for i in range(2)]
        sums = [pb(f"sums{i}", [P, 512], fp32) for i in range(2)]

        raw_in = [[sem(f"raw_in{s}{k}") for k in range(G)] for s in range(2)]
        x_in = [sem(f"x_in{i}") for i in range(2)]
        x_native_in = sem("x_native_in")
        x_hi_by_act = sem("x_hi_by_act")
        x_hi_by_pool = sem("x_hi_by_pool")
        x_lo_by_pool = sem("x_lo_by_pool")
        x_lo_by_dve = sem("x_lo_by_dve")
        xres_in = [sem(f"xres_in{s}") for s in range(2)]
        consts_ready = sem("consts_ready")
        const_step = sem("const_step")
        signs_ready = sem("signs_ready")
        summed = sem("summed")
        count_ready = sem("count_ready")
        norm_ready = sem("norm_ready")
        scaled_ready = sem("scaled_ready")
        inc_ready = sem("inc_ready")
        incT_ready = sem("incT_ready")
        hi_by_act = sem("hi_by_act")
        hi_by_pool = sem("hi_by_pool")
        lo_by_pool = sem("lo_by_pool")
        lo_by_dve = sem("lo_by_dve")
        native_done = sem("native_done")
        edge_ready = sem("edge_ready")
        dve_step = sem("dve_step")
        y_ready = sem("y_ready")
        var_ready = sem("var_ready")
        rstd_ready = sem("rstd_ready")
        result_ready = sem("result_ready")
        stored = [sem(f"stored{s}") for s in range(2)]

        block = ctx.enter_context(nc.Block())

        PAIRS = TILES // 2
        X_AT = [0, B // 4, B // 2, SPLIT]
        ACT_HI = [0, 3]
        POOL_HI = [1, 2]
        STEPS = 5

        def x_stage(c):
            if c == 2:
                return rows[:, 0:X_AT[3] - X_AT[2], :]
            slot = incT[:, 1, :, :, :].rearrange("p b q j -> p (b q j)")
            return slot[:, X_AT[c] * D:X_AT[c + 1] * D].rearrange("p (b d) -> p b d", d=D)

        def x_part(c, h):
            return x_split[:, X_AT[c]:X_AT[c + 1], h, :]

        def hi_of(s, q):
            return inc_hi[:, s, :, q, :]

        @block.sync
        def _(sp):
            def load_quarter(t, s, k, reuse):
                if reuse:
                    sp.wait_ge(inc_ready, G * t - 2 * G + k + 1)
                sp.dma_start(raw[:, s, k, :], adj_v[t, :, :, k, :]).then_inc(raw_in[s][k], 16)

            def load_residual(t, s, reuse):
                if reuse:
                    sp.wait_ge(y_ready, t - 1)
                sp.dma_start(xres[:, s, :], x_rows[t]).then_inc(xres_in[s], 16)

            def store(t, s):
                sp.wait_ge(result_ready, t + 1)
                sp.dma_start(out_rows[t], result[:, s, :]).then_inc(stored[s], 16)

            for k in range(G):
                load_quarter(0, 0, k, False)
            for g in range(G):
                sp.dma_start(incT[SQ * g:SQ * (g + 1), 1, :, :, :].rearrange("p b q j -> p (b q j)"),
                             x_v[g, :, 0:X_AT[2], :]).then_inc(x_in[0], 16)
            for g in range(G):
                sp.dma_start(x_native[SQ * g:SQ * (g + 1), :, :], x_v[g, :, SPLIT:B, :]).then_inc(x_native_in, 16)
            for k in range(G):
                load_quarter(1, 1, k, False)
            for g in range(G):
                sp.dma_start(rows[SQ * g:SQ * (g + 1), 0:SPLIT - X_AT[2], :],
                             x_v[g, :, X_AT[2]:SPLIT, :]).then_inc(x_in[1], 16)
            for s in range(2):
                for k in range(G):
                    load_quarter(2 + s, s, k, True)
                sp.wait_ge(x_lo_by_pool, 2)
                load_residual(s, s, False)
            with sp.Fori(2, PAIRS) as u:
                for s in range(2):
                    t = 2 * u + s
                    for k in range(G):
                        load_quarter(t, s, k, True)
                    store(t - 4, s)
                    load_residual(t - 2, s, True)
            for s in range(2):
                store(TILES - 4 + s, s)
                load_residual(TILES - 2 + s, s, True)
            for s in range(2):
                store(TILES - 2 + s, s)
            for s in range(2):
                sp.wait_ge(stored[s], 16 * PAIRS)

        @block.scalar
        def _(act):
            def sign_quarter(t, s, u, q, first=False, reuse=True):
                act.wait_ge(raw_in[s][q], (u + 1) * 16)
                if not first:
                    act.wait_ge(signs_ready, G * t + q)
                if q == 0 and reuse:
                    act.wait_ge(summed, t - 1)
                nc.scalar.activation(sign_out[:, :], raw[:, s, q, :], ACT.Sign, scale=SIGN_SCALE,
                                     bias=sign_bias[:, 0:1], accum_out=part_sums[:, s, 1, q:q + 1]).then_inc(signs_ready, 1)

            def scale_quarter(t, s, q, reuse):
                if q == 0:
                    act.wait_ge(norm_ready, t + 1)
                if reuse or q >= 2:
                    act.wait_ge(inc_ready, G * t + q - 1)
                nc.scalar.mul(scaled[q % 2][:, :], raw[:, s, q, :], norm[:, s, q:q + 1]).then_inc(scaled_ready, 1)

            def round_quarter(t, s, q, reuse):
                if reuse:
                    act.wait_ge(edge_ready, t - 1)
                act.wait_ge(incT_ready, G * t + q + 1)
                nc.scalar.copy(hi_of(s, q), incT[:, s, 0:SPLIT, q, :]).then_inc(hi_by_act, 1)

            act.wait_ge(consts_ready, 1)
            nc.scalar.activation(table_load[:, :], sign_bias[:, :], ACT.Sign)

            def tile(t, s, u, signs1=True, signs2=True):
                scale_quarter(t, s, 2, True)
                if signs1:
                    sign_quarter(t + 1, 1 - s, u + s, 2)
                    sign_quarter(t + 1, 1 - s, u + s, 3)
                round_quarter(t, s, 0, True)
                scale_quarter(t, s, 3, True)
                if signs2:
                    sign_quarter(t + 2, s, u + 1, 0)
                if signs1:
                    scale_quarter(t + 1, 1 - s, 0, True)
                if signs2:
                    sign_quarter(t + 2, s, u + 1, 1)
                if signs1:
                    scale_quarter(t + 1, 1 - s, 1, True)
                round_quarter(t, s, 3, True)

            for q in range(G):
                sign_quarter(0, 0, 0, q, first=(q == 0), reuse=False)

            def split_x_hi(c):
                act.wait_ge(x_in[c // 2], X_CHUNK)
                nc.scalar.copy(x_part(c, 0), x_stage(c)).then_inc(x_hi_by_act, 1)

            scale_quarter(0, 0, 0, False)
            scale_quarter(0, 0, 1, False)
            scale_quarter(0, 0, 2, False)
            scale_quarter(0, 0, 3, False)
            round_quarter(0, 0, 0, False)
            split_x_hi(1)
            for q in range(3):
                sign_quarter(1, 1, 0, q, reuse=False)
            round_quarter(0, 0, 3, False)
            sign_quarter(1, 1, 0, 3, reuse=False)
            split_x_hi(2)
            scale_quarter(1, 1, 0, True)
            scale_quarter(1, 1, 1, True)
            sign_quarter(2, 0, 1, 0)
            scale_quarter(1, 1, 2, True)
            scale_quarter(1, 1, 3, True)
            sign_quarter(2, 0, 1, 1)
            round_quarter(1, 1, 0, False)
            sign_quarter(2, 0, 1, 2)
            sign_quarter(2, 0, 1, 3)
            round_quarter(1, 1, 3, False)
            scale_quarter(2, 0, 0, True)
            scale_quarter(2, 0, 1, True)
            sign_quarter(3, 1, 1, 0)
            sign_quarter(3, 1, 1, 1)
            with act.Fori(1, PAIRS - 1) as u:
                tile(2 * u, 0, u)
                tile(2 * u + 1, 1, u)
            tile(TILES - 2, 0, PAIRS - 1, signs2=False)
            tile(TILES - 1, 1, PAIRS - 1, signs1=False, signs2=False)

        @block.gpsimd
        def _(pool):
            nc.gpsimd.memset(quad_sum[:, :], 0.0).then_inc(const_step, 1)
            nc.gpsimd.memset(half[:, :], 0.5)
            nc.gpsimd.memset(minus_half[:, :], -0.5)
            nc.gpsimd.memset(sign_bias[:, :], SIGN_BIAS)
            nc.gpsimd.memset(own_quarter[:, :], 0.0).then_inc(const_step, 1)
            pool.wait_ge(const_step, 2)
            for g in range(G):
                v = quad_sum[:, :].rearrange("p (g j) -> p g j", g=G)
                nc.gpsimd.affine_select(out=v, in_=v, compare_op=ALU.not_equal, fill=0.5, base=-SQ * g,
                                        pattern=[[0, G], [-1, SQ]], channel_multiplier=1).then_inc(const_step, 1)
                pool.wait_ge(const_step, 3 + g)
            for g in range(G):
                last = nc.gpsimd.memset(own_quarter[SQ * g:SQ * (g + 1), g:g + 1], 2.0)
            last.then_inc(consts_ready, 1)

            def norm_of(t, s):
                pool.wait_ge(count_ready, t + 1)
                nc.gpsimd.tensor_tensor(norm[:, s, :], count[:, s, :], half[:, :], ALU.pow).then_inc(norm_ready, 1)

            def rstd_of(t, s):
                pool.wait_ge(var_ready, t + 1)
                nc.gpsimd.tensor_tensor(rstd[:, s:s + 1], var_eps[:, s:s + 1], minus_half[:, :],
                                        ALU.pow).then_inc(rstd_ready, 1)

            def low_quarter(t, s, q, reuse=False, behind=None, also=0):
                if reuse:
                    pool.wait_ge(edge_ready, t - 1)
                if behind is not None:
                    pool.wait_ge(incT_ready, G * t + behind + 1)
                if q in ACT_HI:
                    pool.wait_ge(hi_by_act, len(ACT_HI) * t + ACT_HI.index(q) + 1)
                else:
                    pool.wait_ge(hi_by_pool, len(POOL_HI) * t + POOL_HI.index(q) + 1)
                nc.gpsimd.tensor_tensor(inc_lo[:, s, :, q, :], incT[:, s, 0:SPLIT, q, :], hi_of(s, q).bitcast(fp32),
                                        ALU.subtract).then_inc(lo_by_pool, 1 + also)

            def round_quarter(t, s, q):
                nc.gpsimd.tensor_scalar(hi_of(s, q), incT[:, s, 0:SPLIT, q, :], 1.0, 1.0,
                                        ALU.mult, ALU.mult).then_inc(hi_by_pool, 1)

            norm_of(0, 0)
            pool.wait_ge(x_in[0], X_CHUNK)
            nc.gpsimd.tensor_scalar(x_part(0, 0), x_stage(0), 1.0, 1.0, ALU.mult, ALU.mult).then_inc(x_hi_by_pool, 1)
            pool.wait_ge(x_hi_by_pool, 1)
            nc.gpsimd.tensor_tensor(x_part(0, 1), x_stage(0), x_part(0, 0).bitcast(fp32),
                                    ALU.subtract).then_inc(x_lo_by_pool, 1)

            def tile(t, s, reuse=True, more=True):
                if more and reuse:
                    norm_of(t + 1, 1 - s)
                low_quarter(t, s, 0, reuse, behind=1)
                round_quarter(t, s, 1)
                if reuse:
                    rstd_of(t - 2, s)
                else:
                    norm_of(t + 1, 1 - s)
                low_quarter(t, s, 1, behind=2)
                round_quarter(t, s, 2)
                low_quarter(t, s, 2)
                low_quarter(t, s, 3)

            low_quarter(0, 0, 0, behind=2)
            round_quarter(0, 0, 1)
            round_quarter(0, 0, 2)
            low_quarter(0, 0, 1, also=2)
            norm_of(1, 1)
            pool.wait_ge(x_hi_by_act, 2)
            nc.gpsimd.tensor_tensor(x_part(2, 1), x_stage(2), x_part(2, 0).bitcast(fp32),
                                    ALU.subtract).then_inc(x_lo_by_pool, 1)
            tile(1, 1, reuse=False)
            with pool.Fori(1, PAIRS - 1) as u:
                tile(2 * u, 0)
                tile(2 * u + 1, 1)
            tile(TILES - 2, 0)
            tile(TILES - 1, 1, more=False)
            for s in range(2):
                rstd_of(TILES - 2 + s, s)

        @block.vector
        def _(dve):
            def split_x_lo(c):
                dve.wait_ge(x_hi_by_act, 1)
                nc.vector.tensor_tensor(x_part(c, 1), x_stage(c), x_part(c, 0).bitcast(fp32),
                                        ALU.subtract).then_inc(x_lo_by_dve, 1)

            def low_quarter(t, s, q):
                if q in ACT_HI:
                    dve.wait_ge(hi_by_act, ACT_HI.index(q) + 1)
                else:
                    dve.wait_ge(hi_by_pool, POOL_HI.index(q) + 1)
                nc.vector.tensor_tensor(inc_lo[:, s, :, q, :], incT[:, s, 0:SPLIT, q, :], hi_of(s, q).bitcast(fp32),
                                        ALU.subtract).then_inc(lo_by_dve, 1)

            def count_of(t, s):
                dve.wait_ge(summed, t + 1)
                nc.vector.tensor_scalar(count[:, s, :], sums[s][:, G:2 * G], float(N // 2), 1.0,
                                        ALU.add, ALU.max).then_inc(count_ready, 1)

            def inc_quarter(t, s, q, reuse, reuse_deg):
                if reuse:
                    dve.wait_ge(incT_ready, G * t - G + q + 1)
                if reuse_deg and q == 0:
                    dve.wait_ge(summed, t + 1)
                dve.wait_ge(scaled_ready, G * t + q + 1)
                nc.vector.scalar_tensor_tensor(inc[:, q, :], raw[:, s, q, :], 0.0, scaled[q % 2][:, :],
                                               ALU.is_gt, ALU.add,
                                               accum_out=part_sums[:, s, 0, q:q + 1]).then_inc(inc_ready, 1)

            def transpose_quarter(t, s, q, reuse):
                if reuse and q == 0:
                    dve.wait_ge(lo_by_pool, G * t - G)
                    dve.wait_ge(native_done, t - 1)
                dve.wait_ge(inc_ready, G * t + q + 1)
                nc.vector.transpose(incT[:, s, :, q, :],
                                    inc[:, q, :].rearrange("p (b j) -> p b j", j=SQ)).then_inc(incT_ready, 1)

            def residual(t, s, u):
                def step(ins):
                    ins.then_inc(dve_step, 1)

                def after(k):
                    dve.wait_ge(dve_step, STEPS * t + k)

                dve.wait_ge(summed, t + 3)
                step(nc.vector.scalar_tensor_tensor(deg_pick[:, :], sums[s][:, 0:G], 1.0, own_quarter[:, :],
                                                    ALU.mult, ALU.mult, accum_out=deg[:, :]))
                yield
                after(1)
                step(nc.vector.reciprocal(rdeg[:, :], deg[:, :]))
                yield
                dve.wait_ge(edge_ready, t + 1)
                dve.wait_ge(xres_in[s], 16 * (u + 1))
                after(2)
                step(nc.vector.scalar_tensor_tensor(y_main[:, :], edge[s][:, D:2 * D], rdeg[:, :], xres[:, s, :],
                                                    ALU.mult, ALU.add))
                yield
                after(3)
                nc.vector.scalar_tensor_tensor(y[:, s, :], edge[s][:, 0:D], rdeg[:, :], y_main[:, :],
                                               ALU.mult, ALU.add).then_inc(y_ready, 1)
                yield
                dve.wait_ge(y_ready, t + 1)
                step(nc.vector.bn_stats(stats[:, :], y[:, s, :]))
                yield
                after(4)
                nc.vector.tensor_copy(stats_seen[:, :], stats[:, 0:1])
                step(nc.vector.bn_aggr(mean_var[:, s, :], stats[:, :]))
                yield
                after(5)
                nc.vector.tensor_scalar(var_eps[:, s:s + 1], mean_var[:, s, 1:2], EPS, None,
                                        ALU.add).then_inc(var_ready, 1)
                yield

            def normalise(t, s, u, reuse):
                dve.wait_ge(rstd_ready, t + 1)
                if reuse:
                    dve.wait_ge(stored[s], 16 * u)
                nc.vector.tensor_scalar(result[:, s, :], y[:, s, :], mean_var[:, s, 0:1], rstd[:, s:s + 1],
                                        ALU.subtract, ALU.mult).then_inc(result_ready, 1)

            def tile(t, s, u, reuse=True, before=True, reuse_slot=True, norm_before=True, reuse_result=True,
                     more=True, x_chunk=None):
                steps = residual(t - 2, s, u - 1) if before else iter(())
                inc_quarter(t, s, 0, reuse, before)
                next(steps, None)
                if norm_before:
                    normalise(t - 3, 1 - s, u - 2 + s, reuse_result)
                inc_quarter(t, s, 1, reuse, before)
                next(steps, None)
                if x_chunk == 2:
                    dve.wait_ge(x_lo_by_pool, 1)
                    dve.wait_ge(x_lo_by_dve, 1)
                transpose_quarter(t, s, 0, reuse_slot)
                next(steps, None)
                inc_quarter(t, s, 2, reuse, before)
                next(steps, None)
                if more and x_chunk is None:
                    count_of(t + 1, 1 - s)
                transpose_quarter(t, s, 1, reuse_slot)
                next(steps, None)
                inc_quarter(t, s, 3, reuse, before)
                next(steps, None)
                transpose_quarter(t, s, 2, reuse_slot)
                next(steps, None)
                transpose_quarter(t, s, 3, reuse_slot)
                if x_chunk == 2:
                    count_of(t + 1, 1 - s)
                if x_chunk == 1:
                    low_quarter(t, s, 2)
                    low_quarter(t, s, 3)
                    count_of(t + 1, 1 - s)
                    split_x_lo(1)

            count_of(0, 0)
            tile(0, 0, 0, reuse=False, before=False, reuse_slot=False, norm_before=False, x_chunk=1)
            tile(1, 1, 0, before=False, reuse_slot=False, norm_before=False, x_chunk=2)
            tile(2, 0, 1, norm_before=False)
            tile(3, 1, 1, reuse_result=False)
            tile(4, 0, 2, reuse_result=False)
            tile(5, 1, 2)
            with dve.Fori(3, PAIRS - 1) as u:
                tile(2 * u, 0, u)
                tile(2 * u + 1, 1, u)
            tile(TILES - 2, 0, PAIRS - 1)
            tile(TILES - 1, 1, PAIRS - 1, more=False)
            normalise(TILES - 3, 1, PAIRS - 2, True)
            for s in range(2):
                for _ in residual(TILES - 2 + s, s, PAIRS - 1):
                    pass
                normalise(TILES - 2 + s, s, PAIRS - 1, True)

        @block.tensor
        def _(pe):
            def sum_signs(t, s):
                pe.wait_ge(signs_ready, G * t + G)
                nc.tensor.matmul(sums[s][:, G:2 * G], quad_sum[:, :], part_sums[:, s, 1, :],
                                 start=True, stop=True).then_inc(summed, 1)

            def sum_quadrants(t, s, reuse, signs):
                pe.wait_ge(incT_ready, G * t + G)
                if signs:
                    pe.wait_ge(signs_ready, G * t + 3 * G)
                pe.wait_ge(count_ready, t + 1)
                if reuse:
                    pe.wait_ge(dve_step, STEPS * t - 2 * STEPS + 1)
                nc.tensor.matmul(sums[s][:, 0:2 * G], quad_sum[:, :],
                                 part_sums[:, s, :, :].rearrange("p k q -> p (k q)"),
                                 start=True, stop=True).then_inc(summed, 1)

            def native_products(t, s, reuse, first, signs, sums_at):
                pe.wait_ge(incT_ready, G * t + G)
                if reuse:
                    pe.wait_ge(y_ready, t - 1)
                if first:
                    pe.wait_ge(x_native_in, X_CHUNK)
                for n in range(NATIVE):
                    last = nc.tensor.matmul(edge[s][:, 0:D], incT[:, s, SPLIT + n, :, :].rearrange("p q j -> p (q j)"),
                                            x_native[:, n, :], start=(n == 0), stop=False)
                    if n == sums_at:
                        if first:
                            sum_signs(1, 1)
                        else:
                            sum_quadrants(t, s, reuse, signs)
                last.then_inc(native_done, 1)

            def split_products(t, s, b0, b1, first):
                if b0 == 0:
                    pe.wait_ge(lo_by_pool, G * t + G)
                    if first:
                        pe.wait_ge(lo_by_dve, 2)
                for b in range(b0, b1):
                    if first and b in X_AT:
                        if b == X_AT[1]:
                            pe.wait_ge(x_lo_by_dve, 1)
                        else:
                            pe.wait_ge(x_lo_by_pool, 1 + X_AT.index(b) // 2)
                    for c0, c1 in ((0, D), (D, 2 * D)) if b == 0 else ((0, 2 * D),):
                        nc.tensor.matmul(edge[s][:, c0:c1], inc_hi[:, s, b, :, :].rearrange("p q j -> p (q j)"),
                                         x_split[:, b, :, :].rearrange("p h d -> p (h d)")[:, c0:c1],
                                         start=False, stop=False)
                    last = nc.tensor.matmul(edge[s][:, D:2 * D], inc_lo[:, s, b, :, :].rearrange("p q j -> p (q j)"),
                                            x_split[:, b, 0, :], start=False, stop=(b == SPLIT - 1))
                if b1 == SPLIT:
                    last.then_inc(edge_ready, 1)

            pe.wait_ge(consts_ready, 1)
            sum_signs(0, 0)
            SUMS_AT = 3
            FIRST_SUMS_AT = 18

            def tile(t, s, reuse=True, signs=True, first=False):
                native_products(t, s, reuse, first, signs, SUMS_AT if reuse else NATIVE - 1)
                split_products(t, s, 0, FIRST_SUMS_AT if first else SPLIT, first)
                if first:
                    sum_quadrants(t, s, False, True)
                    split_products(t, s, FIRST_SUMS_AT, SPLIT, first)

            tile(0, 0, reuse=False, first=True)
            tile(1, 1, reuse=False)
            with pe.Fori(1, PAIRS - 1) as u:
                for s in range(2):
                    tile(2 * u + s, s)
            tile(TILES - 2, 0, signs=False)
            tile(TILES - 1, 1, signs=False)


_INS = ["x", "adj"]


def kernel(**inputs):
    import numpy as _np
    import concourse.bacc as _bacc
    from concourse import mybir as _mybir
    from concourse.bass_utils import run_bass_kernel_spmd as _run

    nc = _bacc.Bacc("TRN2", target_bir_lowering=False, num_devices=1)
    arrays, args = {}, []
    for name in _INS:
        a = _np.ascontiguousarray(inputs[name])
        arrays[f"in_{name}_dram"] = a
        args.append(nc.dram_tensor(f"in_{name}_dram", a.shape, _mybir.dt.from_np(a.dtype), kind="ExternalInput").ap())
    shape = inputs["x"].shape
    args.append(nc.dram_tensor("out_0_dram", shape, _mybir.dt.float32, kind="ExternalOutput").ap())
    gnn_resnorm_kernel(nc, *args)
    r = _run(nc, [arrays], core_ids=[0])
    return r.results[0]["out_0_dram"]
```
